# Optimizing a Trainium2 kernel written in Bass

```python
import numpy as np
import jax
import jax.numpy as jnp

def _softmax(x, axis=-1):
    return jax.nn.softmax(x, axis=axis)

def _gelu(x):
    return jax.nn.gelu(x, approximate=True)

def _silu(x):
    return jax.nn.silu(x)

def _sigmoid(x):
    return jax.nn.sigmoid(x)

def _layernorm(x, axis=-1, eps=1e-05):
    m = jnp.mean(x, axis=axis, keepdims=True)
    v = jnp.var(x, axis=axis, keepdims=True)
    return (x - m) / jnp.sqrt(v + eps)

def _scatter_add(tgt, idx, src, axis=0):
    return tgt.at[idx].add(src)

def _segment_sum(src, seg, n):
    return jax.ops.segment_sum(src, seg, n)
kernel_name = 'mk_adaln_ffn_d1_seqx_r8_3069ba'

def setup_inputs(seed: int=0):
    np.random.seed(seed)
    _w = jnp.asarray

    def _rec_inputs():
        import jax
        import jax.numpy as jnp
        _rk = jax.random.key(seed)
        x = -8.015e-05 + 0.9999 * jax.random.normal(jax.random.fold_in(_rk, 1), (32, 32, 256), jnp.float32)
        _lenS = 32 - jax.random.randint(jax.random.fold_in(_rk, 7), (32,), 0, max(1, 32 // 4) + 1, jnp.int32)
        _lenS2 = 32 - jax.random.randint(jax.random.fold_in(_rk, 8), (32,), 0, max(1, 32 // 4) + 1, jnp.int32)
        cond_1024 = 0.00191187 + 0.999416 * jax.random.normal(jax.random.fold_in(_rk, 11), (32, 128), jnp.float32)
        return (x, cond_1024)
    x, cond_1024 = _rec_inputs()

    def _L0_cond_setup():
        import jax, jax.numpy as jnp
        import numpy as np
        B, N, V_DIM, Q_DIM = (32, 100, 256, 128)
        key = jax.random.key(seed)
        k1, k2, k3, k4 = jax.random.split(key, 4)
        v = jax.random.normal(k1, (B, N, V_DIM), dtype=jnp.float32)
        q = jax.random.normal(k2, (B, Q_DIM), dtype=jnp.float32)
        W3 = jax.random.normal(k3, (Q_DIM, V_DIM), dtype=jnp.float32) * (1.0 / np.sqrt(Q_DIM))
        b3 = jnp.zeros((V_DIM,), dtype=jnp.float32)
        W2 = jax.random.normal(k4, (V_DIM, V_DIM), dtype=jnp.float32) * (1.0 / np.sqrt(V_DIM))
        b2 = jnp.zeros((V_DIM,), dtype=jnp.float32)
        return {'v': v, 'q': q, 'W3': W3, 'b3': b3, 'W2': W2, 'b2': b2}
    _L0_cond_all = _L0_cond_setup()
    _L0_cond_in = {k: v for k, v in _L0_cond_all.items() if k in ('W3', 'b3', 'W2', 'b2')}
    del _L0_cond_all

    def _L0_ffn_setup():
        import jax, jax.numpy as jnp
        import numpy as np
        D_MODEL = 256
        D_EXPERT = 1024
        EPS = 1e-08

        def ternary_quant(w):
            scale = jnp.mean(jnp.abs(w)) + EPS
            q = jnp.clip(jnp.round(w / scale), -1.0, 1.0) * scale
            return w + jax.lax.stop_gradient(q - w)
        key = jax.random.key(seed)
        k_x, k_up, k_gate, k_down = jax.random.split(key, 4)
        std_in = 1.0 / np.sqrt(D_MODEL)
        std_exp = 1.0 / np.sqrt(D_EXPERT)
        return {'x': jax.random.normal(k_x, (4, 256, D_MODEL), dtype=jnp.float32), 'W_up': jax.random.normal(k_up, (D_EXPERT, D_MODEL), dtype=jnp.float32) * std_in, 'W_gate': jax.random.normal(k_gate, (D_EXPERT, D_MODEL), dtype=jnp.float32) * std_in, 'W_down': jax.random.normal(k_down, (D_MODEL, D_EXPERT), dtype=jnp.float32) * std_exp}
    _L0_ffn_all = _L0_ffn_setup()
    _L0_ffn_in = {k: v for k, v in _L0_ffn_all.items() if k in ('W_up', 'W_gate', 'W_down')}
    del _L0_ffn_all
    return {'x': x, 'cond_1024': cond_1024, 'L0_cond_W3': _L0_cond_in['W3'], 'L0_cond_b3': _L0_cond_in['b3'], 'L0_cond_W2': _L0_cond_in['W2'], 'L0_cond_b2': _L0_cond_in['b2'], 'L0_ffn_W_up': _L0_ffn_in['W_up'], 'L0_ffn_W_gate': _L0_ffn_in['W_gate'], 'L0_ffn_W_down': _L0_ffn_in['W_down']}

def reference(x, cond_1024, L0_cond_W3, L0_cond_b3, L0_cond_W2, L0_cond_b2, L0_ffn_W_up, L0_ffn_W_gate, L0_ffn_W_down):
    import jax
    import jax.numpy as jnp

    def _L0_cond_ref(v, q, W3, b3, W2, b2):
        import jax, jax.numpy as jnp
        import numpy as np
        B, N, V_DIM, Q_DIM = (32, 100, 256, 128)
        q_emb = jax.nn.relu(q @ W3 + b3)
        n = v.shape[1]
        v_sum = jnp.sum(v, axis=1, keepdims=True)
        x = (n * v + v_sum) * q_emb[:, None, :]
        return jax.nn.relu(x @ W2 + b2)

    def _L0_ffn_ref(x, W_up, W_gate, W_down):
        import jax, jax.numpy as jnp
        import numpy as np
        D_MODEL = 256
        D_EXPERT = 1024
        EPS = 1e-08

        def ternary_quant(w):
            scale = jnp.mean(jnp.abs(w)) + EPS
            q = jnp.clip(jnp.round(w / scale), -1.0, 1.0) * scale
            return w + jax.lax.stop_gradient(q - w)
        wu = ternary_quant(W_up)
        wg = ternary_quant(W_gate)
        wd = ternary_quant(W_down)
        up = jnp.einsum('bsd,ed->bse', x, wu)
        gate = jnp.einsum('bsd,ed->bse', x, wg)
        hidden = jax.nn.silu(up) * gate
        return jnp.einsum('bse,de->bsd', hidden, wd)
    x = x + _L0_ffn_ref(_L0_cond_ref(x, cond_1024, L0_cond_W3, L0_cond_b3, L0_cond_W2, L0_cond_b2), L0_ffn_W_up, L0_ffn_W_gate, L0_ffn_W_down)
    return x

_drawn_inputs = setup_inputs


def setup_inputs(seed=0):
    import zlib

    import numpy as np

    out = dict(_drawn_inputs(seed))
    spreads = {'L0_cond_b3': (0.0, 0.1), 'L0_cond_b2': (0.0, 0.8)}
    factors = {}
    for name, (base, spread) in spreads.items():
        noise = np.random.default_rng([zlib.crc32(name.encode()), seed]).standard_normal(out[name].shape)
        drawn = base * np.exp(spread * noise) if base else spread * noise
        out[name] = jnp.asarray(drawn.astype(out[name].dtype))
    for name, factor in factors.items():
        out[name] = (out[name] * factor).astype(out[name].dtype)
    return out
```

```python
import concourse.bass as bass
from concourse import mybir
from contextlib import ExitStack


def adaln_ffn_kernel(nc: bass.Bass, x_t: bass.AP, small: bass.AP, w2: bass.AP,
                     w_up: bass.AP, w_gate: bass.AP, w_down: bass.AP, out: bass.AP):
    f32, f32r, bf16 = mybir.dt.float32, mybir.dt.float32r, mybir.dt.bfloat16
    ALU, ACT, AX = mybir.AluOpType, mybir.ActivationFunctionType, mybir.AxisListType

    P = 128
    NB, NTOK = small.shape[1] - 2 * P - 4, 32
    NQ, DT, QT = x_t.shape[1:]
    BQ = QT // NTOK
    ET = w_up.shape[1]
    HT = 2 * QT
    STEPS = 2 * ET
    LAG = 3
    NW = ET * DT * P
    NCH = 4
    CT = ET // NCH
    COUNT = float(P * NW)
    EPS = 1e-8
    WB = 4
    UP, GATE, DOWN = range(3)
    w_dram = [w_up, w_gate, w_down]

    ctx = ExitStack()
    with ctx:
        def sb(name, shape, dt):
            return ctx.enter_context(nc.sbuf_tensor(name, shape, dt))

        def sem(name):
            return ctx.enter_context(nc.semaphore(name))

        sm = sb("sm", list(small.shape), f32)
        w3_sb = sm[:, 0:2 * P]
        cond_sb = sm[:, 2 * P:2 * P + NB]
        b3_sb = sm[:, 2 * P + NB:2 * P + NB + 2]
        b2_sb = sm[:, 2 * P + NB + 2:2 * P + NB + 4]
        w2_sb = sb("w2_sb", [P, DT, DT * P], f32)
        x_sb = sb("x_sb", [P, NQ, DT, QT], f32)
        w_sb = [sb(f"w_sb{m}", [P, ET, DT, P], f32) for m in range(3)]
        neg = sb("neg", [P, CT, DT, P], bf16)
        neg2 = sb("neg2", [P, CT, DT, P], bf16)
        tern = [sb(f"tern{m}", [P, ET, DT, P], f32r) for m in range(3)]
        ones = sb("ones", [P, P], f32)
        warm = sb("warm", [P, HT], bf16)
        abs_sum = sb("abs_sum", [P, 3, NCH], f32)
        thr = sb("thr", [P, 3, 2], f32)
        scale = sb("scale", [P, 3], f32)
        q_emb = sb("q_emb", [P, DT, NB], f32)
        v_sum = sb("v_sum", [P, DT, NB], f32)
        xc = sb("xc", [P, NQ, DT, QT], f32)
        h = sb("h", [P, DT, NQ, QT], f32)
        h_hi = sb("h_hi", [P, DT, NQ, QT], f32r)
        h_lo = sb("h_lo", [P, DT, NQ, QT], f32r)
        hid = sb("hid", [P, STEPS, HT], f32)
        hid_hi = sb("hid_hi", [P, STEPS, HT], f32r)
        hid_lo = sb("hid_lo", [P, STEPS, HT], f32r)
        y_sb = sb("y_sb", [P, NQ, DT, QT], f32)

        bank = [ctx.enter_context(nc.psum_tensor(f"bank{i}", [P, HT], f32)) for i in range(8)]
        Q_BANK, SUM_BANK, WARM_BANK = 6, 7, 5
        w2_bank = [[0, 1], [2, 3], [4, 5], [4, 5]]
        y_bank = [[4, 5], [6, 7]]

        s_small, s_w2, s_out = sem("s_small"), sem("s_w2"), sem("s_out")
        s_x = [sem(f"s_x{q}") for q in range(NQ)]
        s_w = [[sem(f"s_w{m}_{c}") for c in range(NCH)] for m in range(3)]
        s_const = sem("s_const")
        s_q = sem("s_q")
        s_qemb = sem("s_qemb")
        s_vsum = sem("s_vsum")
        s_xs = sem("s_xs")
        s_xc = sem("s_xc")
        s_hp = sem("s_hp")
        s_h = sem("s_h")
        s_hlo = sem("s_hlo")
        s_abs = sem("s_abs")
        s_sum = sem("s_sum")
        s_thr = sem("s_thr")
        s_neg = sem("s_neg")
        s_tern = sem("s_tern")
        s_up = sem("s_up")
        s_silu = sem("s_silu")
        s_gate = sem("s_gate")
        s_hid = sem("s_hid")
        s_hihi = sem("s_hihi")
        s_hilo = sem("s_hilo")
        s_y = sem("s_y")
        s_fin = sem("s_fin")

        block = ctx.enter_context(nc.Block())

        def chunk(t, c):
            return t[:, c * CT:(c + 1) * CT, :, :]

        def half(t, hf):
            return t[:, 2 * hf:2 * hf + 2, :, :]

        @block.sync
        def _(sp):
            sp.dma_start(sm[:], small).then_inc(s_small, 16)
            sp.dma_start(x_sb[:, 0], x_t[:, 0]).then_inc(s_x[0], 16)
            sp.dma_start(w2_sb[:], w2).then_inc(s_w2, 16)
            sp.dma_start(x_sb[:, 1], x_t[:, 1]).then_inc(s_x[1], 16)
            for c in range(NCH):
                sp.dma_start(chunk(w_sb[UP], c), chunk(w_up, c)).then_inc(s_w[UP][c], 16)
            for q in range(2, NQ):
                sp.dma_start(x_sb[:, q], x_t[:, q]).then_inc(s_x[q], 16)
            for m in (GATE, DOWN):
                for c in range(NCH):
                    sp.dma_start(chunk(w_sb[m], c), chunk(w_dram[m], c)).then_inc(s_w[m][c], 16)
            n = 0
            for hf in range(2):
                for d in range(DT):
                    n += 1
                    sp.wait_ge(s_fin, n)
                    sp.dma_start(half(out, hf)[:, :, d], half(y_sb, hf)[:, :, d]).then_inc(s_out, 16)
            sp.wait_ge(s_out, 16 * n)

        @block.gpsimd
        def _(pool):
            nc.gpsimd.memset(warm[:], 0.0)
            nc.gpsimd.memset(ones[:], 1.0).then_inc(s_const, 1)

        @block.scalar
        def _(act):
            def abs_chunks(m, cs):
                for c in cs:
                    act.wait_ge(s_w[m][c], 16)
                    nc.scalar.activation(chunk(tern[m], c), chunk(w_sb[m], c), ACT.Abs,
                                         accum_out=abs_sum[:, m, c:c + 1]).then_inc(s_abs, 1)

            def h_quarter(q):
                for d in range(DT):
                    act.wait_ge(s_hp, DT * q + d + 1)
                    ps = bank[w2_bank[q][d]][:, 0:QT]
                    nc.scalar.activation(h[:, d, q], ps, ACT.Relu, bias=b2_sb[:, d:d + 1])
                    nc.scalar.activation(h_hi[:, d, q], ps, ACT.Relu, bias=b2_sb[:, d:d + 1]).then_inc(s_h, 1)

            def silu(i):
                act.wait_ge(s_up, i + 1)
                nc.scalar.activation(hid[:, i], bank[i % WB][:, :], ACT.Silu,
                                     scale=scale[:, UP:UP + 1]).then_inc(s_silu, 1)

            act.wait_ge(s_small, 16)
            abs_chunks(UP, range(NCH))
            h_quarter(0)
            h_quarter(1)
            act.wait_ge(s_thr, 1)
            for i in range(4):
                silu(i)
            h_quarter(2)
            silu(4)
            silu(5)
            h_quarter(3)
            silu(6)
            silu(7)
            abs_chunks(GATE, range(NCH))
            for i in range(8, 12):
                silu(i)
            abs_chunks(DOWN, range(NCH))
            for i in range(12, STEPS):
                silu(i)
            for i in range(STEPS):
                act.wait_ge(s_hid, i + 1)
                nc.scalar.activation(hid_hi[:, i], hid[:, i], ACT.Copy).then_inc(s_hihi, 1)

        @block.vector
        def _(dve):
            def x_quarter(q):
                bs = slice(BQ * q, BQ * (q + 1))
                dve.wait_ge(s_x[q], 16)
                xv = x_sb[:, q].rearrange("p d (b n) -> p d b n", n=NTOK)
                nc.vector.tensor_reduce(v_sum[:, :, bs], xv, AX.X, ALU.add).then_inc(s_vsum, 1)
                dve.wait_ge(s_vsum, q + 1)
                for d in range(DT):
                    last = nc.vector.scalar_tensor_tensor(
                        out=xc[:, q, d].rearrange("p (b n) -> p b n", n=NTOK), in0=xv[:, d], scalar=float(NTOK),
                        in1=v_sum[:, d, bs].unsqueeze(2).to_broadcast([P, BQ, NTOK]), op0=ALU.mult, op1=ALU.add)
                last.then_inc(s_xs, 1)
                dve.wait_ge(s_xs, q + 1)
                nc.vector.tensor_tensor(
                    xc[:, q].rearrange("p d (b n) -> p d b n", n=NTOK),
                    xc[:, q].rearrange("p d (b n) -> p d b n", n=NTOK),
                    q_emb[:, :, bs].unsqueeze(3).to_broadcast([P, DT, BQ, NTOK]), ALU.mult).then_inc(s_xc, 1)

            def h_low(q):
                dve.wait_ge(s_h, DT * (q + 1))
                nc.vector.tensor_tensor(h_lo[:, :, q], h[:, :, q], h_hi[:, :, q].bitcast(f32),
                                        ALU.subtract).then_inc(s_hlo, 1)

            def thresholds(m):
                dve.wait_ge(s_sum, m + 1)
                ps = bank[SUM_BANK][:, 0:1]
                nc.vector.tensor_scalar(thr[:, m, 0:1], ps, 0.5 / COUNT, 0.5 * EPS, ALU.mult, ALU.add)
                nc.vector.tensor_scalar(thr[:, m, 1:2], ps, -0.5 / COUNT, -0.5 * EPS, ALU.mult, ALU.add)
                nc.vector.tensor_scalar(scale[:, m:m + 1], ps, 1.0 / COUNT, EPS, ALU.mult,
                                        ALU.add).then_inc(s_thr, 1)
                dve.wait_ge(s_thr, m + 1)

            def ternary(m):
                for c in range(NCH):
                    n = NCH * m + c
                    ng = (neg, neg2)[c % 2]
                    nc.vector.tensor_scalar(ng[:], chunk(w_sb[m], c), thr[:, m, 1:2], None,
                                            ALU.is_lt).then_inc(s_neg, 1)
                    dve.wait_ge(s_neg, n + 1)
                    nc.vector.scalar_tensor_tensor(
                        out=chunk(tern[m], c), in0=chunk(w_sb[m], c), scalar=thr[:, m, 0:1], in1=ng[:],
                        op0=ALU.is_gt, op1=ALU.subtract).then_inc(s_tern, 1)

            dve.wait_ge(s_q, 1)
            for d in range(DT):
                last = nc.vector.tensor_scalar(q_emb[:, d], bank[Q_BANK][:, NB * d:NB * (d + 1)],
                                               b3_sb[:, d:d + 1], 0.0, ALU.add, ALU.max)
            last.then_inc(s_qemb, 1)
            dve.wait_ge(s_qemb, 1)
            x_quarter(0)
            x_quarter(1)
            thresholds(UP)
            ternary(UP)
            h_low(0)
            h_low(1)
            x_quarter(2)
            x_quarter(3)
            h_low(2)
            h_low(3)
            thresholds(GATE)
            ternary(GATE)
            thresholds(DOWN)
            ternary(DOWN)

            def finish(hf):
                for d in range(DT):
                    dve.wait_ge(s_y, DT * hf + d + 1)
                    nc.vector.scalar_tensor_tensor(
                        out=half(y_sb, hf)[:, :, d],
                        in0=bank[y_bank[hf][d]][:, :].rearrange("p (q t) -> p q t", q=2),
                        scalar=scale[:, DOWN:DOWN + 1], in1=half(x_sb, hf)[:, :, d],
                        op0=ALU.mult, op1=ALU.add).then_inc(s_fin, 1)

            def hidden_low(i):
                dve.wait_ge(s_hihi, i + 1)
                nc.vector.tensor_tensor(hid_lo[:, i], hid[:, i], hid_hi[:, i].bitcast(f32),
                                        ALU.subtract).then_inc(s_hilo, 1)

            for i in range(STEPS):
                dve.wait_ge(s_gate, i + 1)
                dve.wait_ge(s_silu, i + 1)
                nc.vector.scalar_tensor_tensor(
                    out=hid[:, i], in0=bank[i % WB][:, :], scalar=scale[:, GATE:GATE + 1], in1=hid[:, i],
                    op0=ALU.mult, op1=ALU.mult).then_inc(s_hid, 1)
                if i:
                    hidden_low(i - 1)
                if i == ET + LAG:
                    finish(0)
            hidden_low(STEPS - 1)
            finish(1)

        @block.tensor
        def _(pe):
            def sum_matrix(m):
                pe.wait_ge(s_abs, NCH * (m + 1))
                if m:
                    pe.wait_ge(s_thr, m)
                for c in range(NCH):
                    last = nc.tensor.matmul(bank[SUM_BANK][:, 0:1], ones[:], abs_sum[:, m, c:c + 1],
                                            start=(c == 0), stop=(c == NCH - 1))
                last.then_inc(s_sum, 1)

            def w2_quarter(q):
                pe.wait_ge(s_xc, q + 1)
                if q == 3:
                    pe.wait_ge(s_h, DT * 3)
                for d in range(DT):
                    for k in range(DT):
                        last = nc.tensor.matmul(bank[w2_bank[q][d]][:, 0:QT], w2_sb[:, k, P * d:P * (d + 1)],
                                                xc[:, q, k], start=(k == 0), stop=(k == DT - 1))
                    last.then_inc(s_hp, 1)

            def h_tile(m, i):
                hf, e = divmod(i, ET)
                qs = slice(2 * hf, 2 * hf + 2)
                n = 0
                for k in range(DT):
                    for part in (h_hi, h_lo):
                        last = nc.tensor.matmul(bank[i % WB][:, :], tern[m][:, e, k],
                                                part[:, k, qs], start=(n == 0), stop=(n == 2 * DT - 1))
                        n += 1
                return last

            def up(i):
                if i == 0:
                    pe.wait_ge(s_hlo, 2)
                if i == ET:
                    pe.wait_ge(s_hlo, 4)
                if i < ET and i % CT == 0:
                    pe.wait_ge(s_tern, i // CT + 1)
                if i >= WB:
                    pe.wait_ge(s_silu, i - WB + 1)
                h_tile(UP, i).then_inc(s_up, 1)

            def gate(i):
                if i < ET and i % CT == 0:
                    pe.wait_ge(s_tern, NCH + i // CT + 1)
                if i < WB:
                    pe.wait_ge(s_silu, STEPS - WB + i + 1)
                else:
                    pe.wait_ge(s_hid, i - WB + 1)
                h_tile(GATE, i).then_inc(s_gate, 1)

            def down(i):
                hf, e = divmod(i, ET)
                if hf == 0 and e % CT == 0:
                    pe.wait_ge(s_tern, 2 * NCH + e // CT + 1)
                pe.wait_ge(s_hilo, i + 1)
                for d in range(DT):
                    for n, part in enumerate((hid_hi, hid_lo)):
                        last = nc.tensor.matmul(bank[y_bank[hf][d]][:, :], tern[DOWN][:, e, d], part[:, i],
                                                start=(e == 0 and n == 0), stop=(e == ET - 1 and n == 1),
                                                )
                    if e == ET - 1:
                        last.then_inc(s_y, 1)

            pe.wait_ge(s_const, 1)
            for _ in range(8):
                nc.tensor.matmul(bank[WARM_BANK][:, :], warm[:, 0:P], warm[:, :], start=True, stop=True)
            pe.wait_ge(s_small, 16)
            for d in range(DT):
                last = nc.tensor.matmul(bank[Q_BANK][:, NB * d:NB * (d + 1)], w3_sb[:, P * d:P * (d + 1)],
                                        cond_sb, start=True, stop=True)
            last.then_inc(s_q, 1)
            pe.wait_ge(s_w2, 16)
            w2_quarter(0)
            w2_quarter(1)
            sum_matrix(UP)
            for i in range(4):
                up(i)
            w2_quarter(2)
            up(4)
            up(5)
            w2_quarter(3)
            up(6)
            up(7)
            for i in range(8, 12):
                up(i)
            sum_matrix(GATE)
            for i in range(12, STEPS):
                up(i)
            sum_matrix(DOWN)
            for i in range(STEPS + LAG):
                if i < STEPS:
                    gate(i)
                if i == LAG:
                    pe.wait_ge(s_thr, 3)
                if i >= LAG:
                    down(i - LAG)


def kernel(x, cond_1024, L0_cond_W3, L0_cond_b3, L0_cond_W2, L0_cond_b2, L0_ffn_W_up, L0_ffn_W_gate, L0_ffn_W_down):
    import numpy as np
    import concourse.bacc as bacc
    from concourse import mybir
    from concourse.bass_utils import run_bass_kernel_spmd

    P, NQ, DT = 128, 4, 2
    B, N, D = x.shape
    E = L0_ffn_W_up.shape[0]
    QT = B * N // NQ
    ET = E // P

    def lay(a):
        return np.ascontiguousarray(a)

    arrays = {
        "x_t": lay(np.asarray(x).reshape(NQ, QT, DT, P).transpose(3, 0, 2, 1)),
        "small": lay(np.concatenate([np.asarray(L0_cond_W3), np.asarray(cond_1024).T,
                                     np.asarray(L0_cond_b3).reshape(DT, P).T,
                                     np.asarray(L0_cond_b2).reshape(DT, P).T], axis=1)),
        "w2": lay(np.asarray(L0_cond_W2).reshape(DT, P, D).transpose(1, 0, 2)),
        "w_up": lay(np.asarray(L0_ffn_W_up).reshape(ET, P, DT, P).transpose(3, 0, 2, 1)),
        "w_gate": lay(np.asarray(L0_ffn_W_gate).reshape(ET, P, DT, P).transpose(3, 0, 2, 1)),
        "w_down": lay(np.asarray(L0_ffn_W_down).reshape(DT, P, ET, P).transpose(3, 2, 0, 1)),
    }
    nc = bacc.Bacc("TRN2", target_bir_lowering=False, num_devices=1)
    args = [nc.dram_tensor(name, a.shape, mybir.dt.from_np(a.dtype), kind="ExternalInput").ap()
            for name, a in arrays.items()]
    y = nc.dram_tensor("y_t", (P, NQ, DT, QT), mybir.dt.float32, kind="ExternalOutput").ap()
    adaln_ffn_kernel(nc, *args, y)
    got = run_bass_kernel_spmd(nc, [arrays], core_ids=[0]).results[0]["y_t"]
    return lay(got.transpose(1, 3, 2, 0)).reshape(B, N, D)
```

```python
import concourse.bass as bass
from concourse import mybir
from contextlib import ExitStack


def adaln_ffn_kernel(nc: bass.Bass, x_t: bass.AP, small: bass.AP, w2: bass.AP,
                     w_up: bass.AP, w_gate: bass.AP, w_down: bass.AP, out: bass.AP):
    f32, f32r, bf16 = mybir.dt.float32, mybir.dt.float32r, mybir.dt.bfloat16
    ALU, ACT, AX = mybir.AluOpType, mybir.ActivationFunctionType, mybir.AxisListType

    P = 128
    NB, NTOK = small.shape[1] - 2 * P - 4, 32
    NQ, DT, QT = x_t.shape[1:]
    BQ = QT // NTOK
    ET = w_up.shape[1]
    HT = 2 * QT
    STEPS = 2 * ET
    LAG = 4
    RING = 8
    NW = ET * DT * P
    NCH = 4
    CT = ET // NCH
    COUNT = float(P * NW)
    EPS = 1e-8
    GB = 3
    WB = 4
    UP, GATE, DOWN = range(3)
    HALVES = [slice(0, 2), slice(2, 4)]
    w_dram = [w_up, w_gate, w_down]

    ctx = ExitStack()
    with ctx:
        def sb(name, shape, dt):
            return ctx.enter_context(nc.sbuf_tensor(name, shape, dt))

        def sem(name):
            return ctx.enter_context(nc.semaphore(name))

        sm = sb("sm", list(small.shape), f32)
        w3_sb = sm[:, 0:2 * P]
        cond_sb = sm[:, 2 * P:2 * P + NB]
        b3_sb = sm[:, 2 * P + NB:2 * P + NB + 2]
        b2_sb = sm[:, 2 * P + NB + 2:2 * P + NB + 4]
        w2_sb = sb("w2_sb", [P, DT, DT * P], f32)
        x_sb = sb("x_sb", [P, NQ, DT, QT], f32)
        w_sb = [sb(f"w_sb{m}", [P, ET, DT, P], f32) for m in range(3)]
        neg = sb("neg", [P, NCH, CT, DT, P], bf16)
        tern = [sb(f"tern{m}", [P, ET, DT, P], f32r) for m in range(3)]
        ones = sb("ones", [P, P], f32)
        warm = sb("warm", [P, HT], bf16)
        w_abs = sb("w_abs", [P, 2, ET, DT, P], f32)
        w_sgn = sb("w_sgn", [P, 2, ET, DT, P], bf16)
        silu_warm = sb("silu_warm", [P, 1], f32)
        abs_sum = sb("abs_sum", [P, 3, NCH], f32)
        w_sum = sb("w_sum", [P, 3], f32)
        thr = sb("thr", [P, 3, 2], f32)
        scale = sb("scale", [P, 3], f32)
        q_emb = sb("q_emb", [P, DT, NB], f32)
        v_sum = sb("v_sum", [P, DT, NB], f32)
        xc = sb("xc", [P, NQ, DT, QT], f32)
        h = sb("h", [P, DT, NQ, QT], f32)
        h_hi = sb("h_hi", [P, DT, NQ, QT], f32r)
        h_lo = sb("h_lo", [P, DT, NQ, QT], f32r)
        hid = sb("hid", [P, STEPS, HT], f32)
        hid_hi = sb("hid_hi", [P, RING, HT], f32r)
        hid_lo = sb("hid_lo", [P, RING, HT], f32r)
        y_sb = sb("y_sb", [P, NQ, DT, QT], f32)

        bank = [ctx.enter_context(nc.psum_tensor(f"bank{i}", [P, HT], f32)) for i in range(8)]
        Q_BANK, SUM_BANK, WARM_BANK = 6, 7, 5
        w2_bank = [[0, 1], [2, 3], [4, 5], [4, 5]]
        pieces = [[(4, 0, 0, 2), (5, 1, 0, 2)], [(6, 0, 2, 4), (7, 1, 2, 3), (3, 1, 3, 4)]]

        s_small, s_w2, s_out = sem("s_small"), sem("s_w2"), sem("s_out")
        s_x = [sem(f"s_x{q}") for q in range(NQ)]
        s_w = [[sem(f"s_w{m}_{c}") for c in range(NCH)] for m in range(3)]
        s_const = sem("s_const")
        s_q = sem("s_q")
        s_qemb = sem("s_qemb")
        s_vsum = sem("s_vsum")
        s_xs = sem("s_xs")
        s_xc = sem("s_xc")
        s_hp = sem("s_hp")
        s_h = sem("s_h")
        s_hhi_first = sem("s_hhi_first")
        s_hhi = sem("s_hhi")
        s_hlo = sem("s_hlo")
        s_abs = sem("s_abs")
        s_abs_last = sem("s_abs_last")
        s_wsum = sem("s_wsum")
        s_sum = sem("s_sum")
        s_thr = sem("s_thr")
        s_neg = sem("s_neg")
        s_tern = sem("s_tern")
        s_up = sem("s_up")
        s_silu = sem("s_silu")
        s_gate = sem("s_gate")
        s_hid = sem("s_hid")
        s_hihi = sem("s_hihi")
        s_hilo = sem("s_hilo")
        s_sgn = sem("s_sgn")
        s_down = sem("s_down")
        s_y = sem("s_y")
        s_fin = sem("s_fin")

        block = ctx.enter_context(nc.Block())

        def chunk(t, c):
            return t[:, c * CT:(c + 1) * CT, :, :]

        @block.sync
        def _(sp):
            sp.dma_start(x_sb[:, 0], x_t[:, 0]).then_inc(s_x[0], 16)
            sp.dma_start(sm[:], small).then_inc(s_small, 16)
            sp.dma_start(w2_sb[:], w2).then_inc(s_w2, 16)
            sp.dma_start(x_sb[:, 1], x_t[:, 1]).then_inc(s_x[1], 16)
            for c in range(NCH):
                sp.dma_start(chunk(w_sb[UP], c), chunk(w_up, c)).then_inc(s_w[UP][c], 16)
            for q in range(2, NQ):
                sp.dma_start(x_sb[:, q], x_t[:, q]).then_inc(s_x[q], 16)
            for m in (GATE, DOWN):
                for c in range(NCH):
                    sp.dma_start(chunk(w_sb[m], c), chunk(w_dram[m], c)).then_inc(s_w[m][c], 16)
            n = 0
            for _, d, q0, q1 in pieces[0] + pieces[1]:
                n += 1
                sp.wait_ge(s_fin, n)
                sp.dma_start(out[:, q0:q1, d], y_sb[:, q0:q1, d]).then_inc(s_out, 16)
            sp.wait_ge(s_out, 16 * n)

        @block.gpsimd
        def _(pool):
            nc.gpsimd.memset(warm[:], 0.0)
            nc.gpsimd.memset(ones[:], 1.0).then_inc(s_const, 1)
            for m in (GATE, DOWN):
                for c in range(NCH):
                    pool.wait_ge(s_w[m][c], 16)
                    nc.gpsimd.tensor_scalar(chunk(w_sgn[:, m - 1], c), chunk(w_sb[m], c), 0.0, -0.5,
                                            ALU.is_ge, ALU.add).then_inc(s_sgn, 1)

        @block.scalar
        def _(act):
            def abs_chunks(m, cs):
                for c in cs:
                    act.wait_ge(s_w[m][c], 16)
                    nc.scalar.activation(chunk(w_abs[:, m - 1] if m else tern[m], c), chunk(w_sb[m], c), ACT.Abs,
                                         accum_out=abs_sum[:, m, c:c + 1]).then_inc(s_abs, 1)

            def h_quarter(q):
                for d in range(DT):
                    act.wait_ge(s_hp, DT * q + d + 1)
                    nc.scalar.activation(h[:, d, q], bank[w2_bank[q][d]][:, 0:QT], ACT.Relu,
                                         bias=b2_sb[:, d:d + 1]).then_inc(s_h, 1)

            def h_high_quarter(q):
                for d in range(DT):
                    nc.scalar.activation(h_hi[:, d, q], bank[w2_bank[q][d]][:, 0:QT], ACT.Relu,
                                         bias=b2_sb[:, d:d + 1]).then_inc(s_hhi_first, 1)

            def silu(i):
                act.wait_ge(s_up, i + 1)
                nc.scalar.activation(hid[:, i], bank[i % WB][:, :], ACT.Silu,
                                     scale=scale[:, UP:UP + 1]).then_inc(s_silu, 1)

            act.wait_ge(s_const, 1)
            nc.scalar.activation(silu_warm[:], warm[:, 0:1], ACT.Silu)
            abs_chunks(UP, range(NCH - 1))
            act.wait_ge(s_small, 16)
            h_quarter(0)
            h_high_quarter(0)
            h_quarter(1)
            h_high_quarter(1)
            abs_chunks(GATE, range(NCH))
            act.wait_ge(s_thr, UP + 1)
            silu(0)
            silu(1)
            abs_chunks(DOWN, [0])
            silu(2)
            silu(3)
            h_quarter(2)
            silu(4)
            abs_chunks(DOWN, [1])
            silu(5)
            h_quarter(3)
            abs_chunks(DOWN, [2])
            silu(6)
            silu(7)
            abs_chunks(DOWN, [3])
            for i in range(ET, STEPS):
                silu(i)
            for i in range(STEPS):
                act.wait_ge(s_hid, i + 1)
                if i >= RING:
                    if i - RING == ET - 1:
                        act.wait_ge(s_y, len(pieces[0]))
                    else:
                        act.wait_ge(s_down, i - RING + 1)
                nc.scalar.activation(hid_hi[:, i % RING], hid[:, i], ACT.Copy).then_inc(s_hihi, 1)

        @block.vector
        def _(dve):
            def x_quarter(q):
                bs = slice(BQ * q, BQ * (q + 1))
                dve.wait_ge(s_x[q], 16)
                xv = x_sb[:, q].rearrange("p d (b n) -> p d b n", n=NTOK)
                nc.vector.tensor_reduce(v_sum[:, :, bs], xv, AX.X, ALU.add).then_inc(s_vsum, 1)
                dve.wait_ge(s_vsum, q + 1)
                for d in range(DT):
                    last = nc.vector.scalar_tensor_tensor(
                        out=xc[:, q, d].rearrange("p (b n) -> p b n", n=NTOK), in0=xv[:, d], scalar=float(NTOK),
                        in1=v_sum[:, d, bs].unsqueeze(2).to_broadcast([P, BQ, NTOK]), op0=ALU.mult, op1=ALU.add)
                last.then_inc(s_xs, 1)
                if q == 0:
                    query_embedding()
                dve.wait_ge(s_xs, q + 1)
                nc.vector.tensor_tensor(
                    xc[:, q].rearrange("p d (b n) -> p d b n", n=NTOK),
                    xc[:, q].rearrange("p d (b n) -> p d b n", n=NTOK),
                    q_emb[:, :, bs].unsqueeze(3).to_broadcast([P, DT, BQ, NTOK]), ALU.mult).then_inc(s_xc, 1)

            def split_h(q):
                if q < 2:
                    dve.wait_ge(s_hhi_first, DT * (q + 1))
                else:
                    dve.wait_ge(s_h, DT * (q + 1))
                    nc.vector.tensor_copy(h_hi[:, :, q], h[:, :, q]).then_inc(s_hhi, 1)
                    dve.wait_ge(s_hhi, q - 1)
                nc.vector.tensor_tensor(h_lo[:, :, q], h[:, :, q], h_hi[:, :, q].bitcast(f32),
                                        ALU.subtract).then_inc(s_hlo, 1)

            def thresholds(m):
                dve.wait_ge(s_sum, m + 1)
                nc.vector.tensor_reduce(w_sum[:, m:m + 1], bank[SUM_BANK][:, 0:NCH], AX.X,
                                        ALU.add).then_inc(s_wsum, 1)
                dve.wait_ge(s_wsum, m + 1)
                ps = w_sum[:, m:m + 1]
                nc.vector.tensor_scalar(thr[:, m, 0:1], ps, 0.5 / COUNT, 0.5 * EPS, ALU.mult, ALU.add)
                if m == UP:
                    nc.vector.tensor_scalar(thr[:, m, 1:2], ps, -0.5 / COUNT, -0.5 * EPS, ALU.mult, ALU.add)
                k = 1.0 if m == UP else 2.0
                nc.vector.tensor_scalar(scale[:, m:m + 1], ps, k / COUNT, k * EPS, ALU.mult,
                                        ALU.add).then_inc(s_thr, 1)
                dve.wait_ge(s_thr, m + 1)

            def negative_up(c):
                nc.vector.tensor_scalar(neg[:, c], chunk(w_sb[UP], c), thr[:, UP, 1:2], None,
                                        ALU.is_lt).then_inc(s_neg, 1)

            def ternary(m, c):
                if m == UP:
                    dve.wait_ge(s_neg, c + 1)
                    nc.vector.scalar_tensor_tensor(
                        out=chunk(tern[m], c), in0=chunk(w_sb[m], c), scalar=thr[:, m, 0:1], in1=neg[:, c],
                        op0=ALU.is_gt, op1=ALU.subtract).then_inc(s_tern, 1)
                else:
                    dve.wait_ge(s_sgn, NCH * (m - 1) + c + 1)
                    nc.vector.scalar_tensor_tensor(
                        out=chunk(tern[m], c), in0=chunk(w_abs[:, m - 1], c), scalar=thr[:, m, 0:1],
                        in1=chunk(w_sgn[:, m - 1], c), op0=ALU.is_gt, op1=ALU.mult).then_inc(s_tern, 1)

            def query_embedding():
                dve.wait_ge(s_q, 1)
                for d in range(DT):
                    last = nc.vector.tensor_scalar(q_emb[:, d], bank[Q_BANK][:, NB * d:NB * (d + 1)],
                                                   b3_sb[:, d:d + 1], 0.0, ALU.add, ALU.max)
                last.then_inc(s_qemb, 1)
                dve.wait_ge(s_qemb, 1)

            def finish(hf):
                for n, (b, d, q0, q1) in enumerate(pieces[hf]):
                    dve.wait_ge(s_y, len(pieces[0]) * hf + n + 1)
                    nc.vector.scalar_tensor_tensor(
                        out=y_sb[:, q0:q1, d],
                        in0=bank[b][:, 0:QT * (q1 - q0)].rearrange("p (q t) -> p q t", t=QT),
                        scalar=scale[:, DOWN:DOWN + 1], in1=x_sb[:, q0:q1, d],
                        op0=ALU.mult, op1=ALU.add).then_inc(s_fin, 1)

            def hidden_low(i):
                dve.wait_ge(s_hihi, i + 1)
                nc.vector.tensor_tensor(hid_lo[:, i % RING], hid[:, i], hid_hi[:, i % RING].bitcast(f32),
                                        ALU.subtract).then_inc(s_hilo, 1)

            def hidden(i):
                dve.wait_ge(s_gate, i + 1)
                dve.wait_ge(s_silu, i + 1)
                nc.vector.scalar_tensor_tensor(
                    out=hid[:, i], in0=bank[i % GB][:, :], scalar=scale[:, GATE:GATE + 1], in1=hid[:, i],
                    op0=ALU.mult, op1=ALU.mult).then_inc(s_hid, 1)

            x_quarter(0)
            x_quarter(1)
            dve.wait_ge(s_w[UP][NCH - 1], 16)
            nc.vector.tensor_reduce(abs_sum[:, UP, NCH - 1:NCH], chunk(w_sb[UP], NCH - 1), AX.XYZ, ALU.add,
                                    apply_absolute_value=True).then_inc(s_abs_last, 1)
            thresholds(UP)
            negative_up(0)
            split_h(0)
            ternary(UP, 0)
            negative_up(1)
            split_h(1)
            ternary(UP, 1)
            negative_up(2)
            x_quarter(2)
            ternary(UP, 2)
            negative_up(3)
            x_quarter(3)
            ternary(UP, 3)
            split_h(2)
            thresholds(GATE)
            for c in range(NCH - 1):
                ternary(GATE, c)
            split_h(3)
            ternary(GATE, NCH - 1)
            thresholds(DOWN)
            for c in range(NCH):
                ternary(DOWN, c)
            for i in range(STEPS):
                hidden(i)
                if i:
                    hidden_low(i - 1)
                if i == ET + LAG:
                    finish(0)
            hidden_low(STEPS - 1)
            finish(1)

        @block.tensor
        def _(pe):
            def sum_matrix(m):
                pe.wait_ge(s_abs, NCH * (m + 1) - 1)
                if m == UP:
                    pe.wait_ge(s_abs_last, 1)
                if m:
                    pe.wait_ge(s_thr, m)
                nc.tensor.matmul(bank[SUM_BANK][:, 0:NCH], ones[:], abs_sum[:, m], start=True,
                                 stop=True).then_inc(s_sum, 1)

            def w2_quarter(q):
                pe.wait_ge(s_xc, q + 1)
                if q == 3:
                    pe.wait_ge(s_h, DT * 3)
                for d in range(DT):
                    for k in range(DT):
                        last = nc.tensor.matmul(bank[w2_bank[q][d]][:, 0:QT], w2_sb[:, k, P * d:P * (d + 1)],
                                                xc[:, q, k], start=(k == 0), stop=(k == DT - 1))
                    last.then_inc(s_hp, 1)

            def h_tile(m, i, out, qs):
                n = 0
                for k in range(DT):
                    for part in (h_hi, h_lo):
                        last = nc.tensor.matmul(out, tern[m][:, i % ET, k], part[:, k, qs],
                                                start=(n == 0), stop=(n == 2 * DT - 1))
                        n += 1
                return last

            def up(i):
                if i == ET:
                    pe.wait_ge(s_hlo, 4)
                if i < ET and i % CT == 0:
                    pe.wait_ge(s_tern, i // CT + 1)
                if i >= WB:
                    pe.wait_ge(s_silu, i - WB + 1)
                h_tile(UP, i, bank[i % WB][:, :], HALVES[i // ET]).then_inc(s_up, 1)

            def gate(i):
                if i < ET and i % CT == 0:
                    pe.wait_ge(s_tern, NCH + i // CT + 1)
                if i < GB:
                    pe.wait_ge(s_silu, STEPS - WB + i + 1)
                else:
                    pe.wait_ge(s_hid, i - GB + 1)
                h_tile(GATE, i, bank[i % GB][:, :], HALVES[i // ET]).then_inc(s_gate, 1)

            def down(i, n):
                hf, e = divmod(i, ET)
                b, d, q0, q1 = pieces[hf][n]
                if n == 0:
                    pe.wait_ge(s_hilo, i + 1)
                    if hf == 0 and e % CT == 0:
                        pe.wait_ge(s_tern, 2 * NCH + e // CT + 1)
                if b < WB and e == 0:
                    pe.wait_ge(s_silu, STEPS)
                ts = slice(QT * (q0 % 2), QT * (q0 % 2 + q1 - q0))
                for k, part in enumerate((hid_hi, hid_lo)):
                    last = nc.tensor.matmul(bank[b][:, 0:QT * (q1 - q0)], tern[DOWN][:, e, d],
                                            part[:, i % RING, ts], start=(e == 0 and k == 0),
                                            stop=(e == ET - 1 and k == 1))
                if e == ET - 1:
                    last.then_inc(s_y, 1)
                elif n == len(pieces[hf]) - 1:
                    last.then_inc(s_down, 1)

            def warm_up():
                nc.tensor.matmul(bank[WARM_BANK][:, :], warm[:, 0:P], warm[:, :], start=True, stop=True)

            pe.wait_ge(s_const, 1)
            for _ in range(6):
                warm_up()
            pe.wait_ge(s_small, 16)
            for d in range(DT):
                last = nc.tensor.matmul(bank[Q_BANK][:, NB * d:NB * (d + 1)], w3_sb[:, P * d:P * (d + 1)],
                                        cond_sb, start=True, stop=True)
            last.then_inc(s_q, 1)
            for _ in range(4):
                warm_up()
            pe.wait_ge(s_w2, 16)
            w2_quarter(0)
            sum_matrix(UP)
            w2_quarter(1)
            for _ in range(4):
                warm_up()
            for q in range(2):
                pe.wait_ge(s_hlo, q + 1)
                pe.wait_ge(s_tern, 1)
                for i in range(2):
                    last = h_tile(UP, i, bank[i % WB][:, QT * q:QT * (q + 1)], q)
                    if q:
                        last.then_inc(s_up, 1)
            up(2)
            up(3)
            w2_quarter(2)
            up(4)
            up(5)
            sum_matrix(GATE)
            w2_quarter(3)
            up(6)
            up(7)
            for i in range(8, STEPS):
                up(i)
                if i == 9:
                    sum_matrix(DOWN)
            for i in range(STEPS):
                gate(i)
                if i >= LAG:
                    for n in range(len(pieces[(i - LAG) // ET])):
                        down(i - LAG, n)
            for n in range(len(pieces[1])):
                for i in range(STEPS - LAG, STEPS):
                    down(i, n)


def kernel(x, cond_1024, L0_cond_W3, L0_cond_b3, L0_cond_W2, L0_cond_b2, L0_ffn_W_up, L0_ffn_W_gate, L0_ffn_W_down):
    import numpy as np
    import concourse.bacc as bacc
    from concourse import mybir
    from concourse.bass_utils import run_bass_kernel_spmd

    P, NQ, DT = 128, 4, 2
    B, N, D = x.shape
    E = L0_ffn_W_up.shape[0]
    QT = B * N // NQ
    ET = E // P

    def lay(a):
        return np.ascontiguousarray(a)

    arrays = {
        "x_t": lay(np.asarray(x).reshape(NQ, QT, DT, P).transpose(3, 0, 2, 1)),
        "small": lay(np.concatenate([np.asarray(L0_cond_W3), np.asarray(cond_1024).T,
                                     np.asarray(L0_cond_b3).reshape(DT, P).T,
                                     np.asarray(L0_cond_b2).reshape(DT, P).T], axis=1)),
        "w2": lay(np.asarray(L0_cond_W2).reshape(DT, P, D).transpose(1, 0, 2)),
        "w_up": lay(np.asarray(L0_ffn_W_up).reshape(ET, P, DT, P).transpose(3, 0, 2, 1)),
        "w_gate": lay(np.asarray(L0_ffn_W_gate).reshape(ET, P, DT, P).transpose(3, 0, 2, 1)),
        "w_down": lay(np.asarray(L0_ffn_W_down).reshape(DT, P, ET, P).transpose(3, 2, 0, 1)),
    }
    nc = bacc.Bacc("TRN2", target_bir_lowering=False, num_devices=1)
    args = [nc.dram_tensor(name, a.shape, mybir.dt.from_np(a.dtype), kind="ExternalInput").ap()
            for name, a in arrays.items()]
    y = nc.dram_tensor("y_t", (P, NQ, DT, QT), mybir.dt.float32, kind="ExternalOutput").ap()
    adaln_ffn_kernel(nc, *args, y)
    got = run_bass_kernel_spmd(nc, [arrays], core_ids=[0]).results[0]["y_t"]
    return lay(got.transpose(1, 3, 2, 0)).reshape(B, N, D)
```

```python
import concourse.bass as bass
from concourse import mybir
from contextlib import ExitStack


def adaln_ffn_kernel(nc: bass.Bass, x_t: bass.AP, small: bass.AP, w2: bass.AP,
                     w_up: bass.AP, w_gate: bass.AP, w_down: bass.AP, out: bass.AP):
    f32, f32r, bf16 = mybir.dt.float32, mybir.dt.float32r, mybir.dt.bfloat16
    ALU, ACT, AX = mybir.AluOpType, mybir.ActivationFunctionType, mybir.AxisListType

    P = 128
    NB, NTOK = small.shape[1] - 2 * P - 4, 32
    NQ, DT, QT = x_t.shape[1:]
    BQ = QT // NTOK
    ET = w_up.shape[1]
    HT = 2 * QT
    STEPS = 2 * ET
    LAG = 4
    RING = 8
    NW = ET * DT * P
    NCH = 4
    CT = ET // NCH
    COUNT = float(P * NW)
    EPS = 1e-8
    WB = 4
    UP, GATE, DOWN = range(3)
    HALVES = [slice(0, 2), slice(2, 4)]
    w_dram = [w_up, w_gate, w_down]

    ctx = ExitStack()
    with ctx:
        def sb(name, shape, dt):
            return ctx.enter_context(nc.sbuf_tensor(name, shape, dt))

        def sem(name):
            return ctx.enter_context(nc.semaphore(name))

        sm = sb("sm", list(small.shape), f32)
        w3_sb = sm[:, 0:2 * P]
        cond_sb = sm[:, 2 * P:2 * P + NB]
        b3_sb = sm[:, 2 * P + NB:2 * P + NB + 2]
        b2_sb = sm[:, 2 * P + NB + 2:2 * P + NB + 4]
        w2_sb = sb("w2_sb", [P, DT, DT * P], f32)
        x_sb = sb("x_sb", [P, NQ, DT, QT], f32)
        w_sb = [sb(f"w_sb{m}", [P, ET, DT, P], f32) for m in range(3)]
        neg = sb("neg", [P, NCH, CT, DT, P], bf16)
        tern = [sb(f"tern{m}", [P, ET, DT, P], f32r) for m in range(3)]
        ones = sb("ones", [P, P], f32)
        warm = sb("warm", [P, HT], bf16)
        w_abs = [sb(f"w_abs{m}", [P, ET, DT, P], f32) for m in (UP, GATE)]
        w_sgn = [sb(f"w_sgn{m}", [P, ET, DT, P], bf16) for m in (UP, GATE)]
        silu_warm = sb("silu_warm", [P, 1], f32)
        abs_sum = sb("abs_sum", [P, 3, NCH], f32)
        w_sum = sb("w_sum", [P, 3], f32)
        thr = sb("thr", [P, 3, 2], f32)
        scale = sb("scale", [P, 3], f32)
        q_emb = sb("q_emb", [P, DT, NB], f32)
        v_sum = sb("v_sum", [P, DT, NB], f32)
        xc = sb("xc", [P, NQ, DT, QT], f32)
        h = sb("h", [P, DT, NQ, QT], f32)
        h_hi = sb("h_hi", [P, DT, NQ, QT], f32r)
        h_lo = sb("h_lo", [P, DT, NQ, QT], f32r)
        hid = sb("hid", [P, STEPS, HT], f32)
        hid_hi = sb("hid_hi", [P, RING, HT], f32r)
        hid_lo = sb("hid_lo", [P, RING, HT], f32r)
        y_sb = sb("y_sb", [P, NQ, DT, QT], f32)

        psum = ctx.enter_context(nc.psum_tensor("psum", [P, 8, HT], f32))
        bank = [psum[:, b, :] for b in range(8)]
        Q_BANK, SUM_BANK, WARM_BANK = 6, 7, 5
        w2_bank = [[0, 1], [2, 3], [4, 5], [6, 4]]
        pieces = [[(4, 0, 0, 2), (5, 1, 0, 2)], [(6, 0, 2, 4), (7, 1, 2, 3), (4, 1, 3, 4)]]

        s_small, s_w2, s_out = sem("s_small"), sem("s_w2"), sem("s_out")
        s_x = [sem(f"s_x{q}") for q in range(NQ)]
        s_w = [[sem(f"s_w{m}_{c}") for c in range(NCH)] for m in range(3)]
        s_const = sem("s_const")
        s_q = sem("s_q")
        s_qemb = sem("s_qemb")
        s_vsum = sem("s_vsum")
        s_xs = sem("s_xs")
        s_xc = sem("s_xc")
        s_hp = sem("s_hp")
        s_h = sem("s_h")
        s_hhi_first = sem("s_hhi_first")
        s_hhi = sem("s_hhi")
        s_hlo = sem("s_hlo")
        s_abs = sem("s_abs")
        s_abs_last = sem("s_abs_last")
        s_wsum = sem("s_wsum")
        s_sum = sem("s_sum")
        s_thr = sem("s_thr")
        s_scale = sem("s_scale")
        s_neg = sem("s_neg")
        s_tern = sem("s_tern")
        s_up = sem("s_up")
        s_silu = sem("s_silu")
        s_gate = sem("s_gate")
        s_hid = sem("s_hid")
        s_hihi = sem("s_hihi")
        s_hilo = sem("s_hilo")
        s_sgn = sem("s_sgn")
        s_down = sem("s_down")
        s_y = sem("s_y")
        s_fin = sem("s_fin")

        block = ctx.enter_context(nc.Block())

        def chunk(t, c):
            return t[:, c * CT:(c + 1) * CT, :, :]

        @block.sync
        def _(sp):
            sp.dma_start(x_sb[:, 0], x_t[:, 0]).then_inc(s_x[0], 16)
            sp.dma_start(sm[:], small).then_inc(s_small, 16)
            sp.dma_start(w2_sb[:], w2).then_inc(s_w2, 16)
            sp.dma_start(x_sb[:, 1], x_t[:, 1]).then_inc(s_x[1], 16)
            for c in range(NCH):
                sp.dma_start(chunk(w_sb[UP], c), chunk(w_up, c)).then_inc(s_w[UP][c], 16)
            for q in range(2, NQ):
                sp.dma_start(x_sb[:, q], x_t[:, q]).then_inc(s_x[q], 16)
            for m in (GATE, DOWN):
                for c in range(NCH):
                    sp.dma_start(chunk(w_sb[m], c), chunk(w_dram[m], c)).then_inc(s_w[m][c], 16)
            n = 0
            for _, d, q0, q1 in pieces[0] + pieces[1]:
                n += 1
                sp.wait_ge(s_fin, n)
                sp.dma_start(out[:, q0:q1, d], y_sb[:, q0:q1, d]).then_inc(s_out, 16)
            sp.wait_ge(s_out, 16 * n)

        @block.gpsimd
        def _(pool):
            nc.gpsimd.memset(warm[:], 0.0)
            nc.gpsimd.memset(ones[:], 1.0).then_inc(s_const, 1)
            for m in (UP, GATE):
                for c in range(NCH):
                    pool.wait_ge(s_w[m][c], 16)
                    nc.gpsimd.tensor_scalar(chunk(w_sgn[m], c), chunk(w_sb[m], c), 0.0, -0.5,
                                            ALU.is_ge, ALU.add).then_inc(s_sgn, 1)

        @block.scalar
        def _(act):
            def abs_chunks(m, cs):
                for c in cs:
                    act.wait_ge(s_w[m][c], 16)
                    out = chunk(tern[m] if m == DOWN else w_abs[m], c)
                    if (m, c) == (UP, NCH - 1):
                        nc.scalar.activation(out, chunk(w_sb[m], c), ACT.Abs).then_inc(s_abs, 1)
                    else:
                        nc.scalar.activation(out, chunk(w_sb[m], c), ACT.Abs,
                                             accum_out=abs_sum[:, m, c:c + 1]).then_inc(s_abs, 1)

            def h_quarter(q):
                for d in range(DT):
                    ps = psum[:, w2_bank[q][d], 0:QT]
                    act.wait_ge(s_hp, DT * q + d + 1)
                    nc.scalar.activation(h[:, d, q], ps, ACT.Relu, bias=b2_sb[:, d:d + 1]).then_inc(s_h, 1)
                    if q < 2:
                        nc.scalar.activation(h_hi[:, d, q], ps, ACT.Relu,
                                             bias=b2_sb[:, d:d + 1]).then_inc(s_hhi_first, 1)

            def silu(i):
                act.wait_ge(s_up, i + 1)
                nc.scalar.activation(hid[:, i], psum[:, i % WB], ACT.Silu,
                                     scale=scale[:, UP:UP + 1]).then_inc(s_silu, 1)

            act.wait_ge(s_const, 1)
            nc.scalar.activation(silu_warm[:], warm[:, 0:1], ACT.Silu)
            abs_chunks(UP, range(NCH - 1))
            act.wait_ge(s_small, 16)
            h_quarter(0)
            h_quarter(1)
            abs_chunks(UP, [NCH - 1])
            abs_chunks(GATE, range(NCH))
            act.wait_ge(s_scale, UP + 1)
            silu(0)
            silu(1)
            abs_chunks(DOWN, [0])
            silu(2)
            silu(3)
            h_quarter(2)
            abs_chunks(DOWN, [1])
            silu(4)
            h_quarter(3)
            silu(5)
            abs_chunks(DOWN, [2])
            silu(6)
            silu(7)
            abs_chunks(DOWN, [3])
            with act.Fori(ET, STEPS) as i:
                silu(i)

            def hidden_high(i):
                act.wait_ge(s_hid, i + 1)
                nc.scalar.activation(hid_hi[:, i % RING], hid[:, i], ACT.Copy).then_inc(s_hihi, 1)

            with act.Fori(0, RING) as i:
                hidden_high(i)
            with act.Fori(RING, STEPS) as i:
                act.wait_ge(s_down, i - (RING - 1))
                hidden_high(i)

        @block.vector
        def _(dve):
            def x_quarter(q):
                bs = slice(BQ * q, BQ * (q + 1))
                dve.wait_ge(s_x[q], 16)
                xv = x_sb[:, q].rearrange("p d (b n) -> p d b n", n=NTOK)
                nc.vector.tensor_reduce(v_sum[:, :, bs], xv, AX.X, ALU.add).then_inc(s_vsum, 1)
                dve.wait_ge(s_vsum, q + 1)
                for d in range(DT):
                    last = nc.vector.scalar_tensor_tensor(
                        out=xc[:, q, d].rearrange("p (b n) -> p b n", n=NTOK), in0=xv[:, d], scalar=float(NTOK),
                        in1=v_sum[:, d, bs].unsqueeze(2).to_broadcast([P, BQ, NTOK]), op0=ALU.mult, op1=ALU.add)
                last.then_inc(s_xs, 1)
                if q == 0:
                    query_embedding()
                dve.wait_ge(s_xs, q + 1)
                nc.vector.tensor_tensor(
                    xc[:, q].rearrange("p d (b n) -> p d b n", n=NTOK),
                    xc[:, q].rearrange("p d (b n) -> p d b n", n=NTOK),
                    q_emb[:, :, bs].unsqueeze(3).to_broadcast([P, DT, BQ, NTOK]), ALU.mult).then_inc(s_xc, 1)

            def split_h(q):
                if q < 2:
                    dve.wait_ge(s_hhi_first, DT * (q + 1))
                else:
                    dve.wait_ge(s_h, DT * (q + 1))
                    nc.vector.tensor_copy(h_hi[:, :, q], h[:, :, q]).then_inc(s_hhi, 1)
                    dve.wait_ge(s_hhi, q - 1)
                nc.vector.tensor_tensor(h_lo[:, :, q], h[:, :, q], h_hi[:, :, q].bitcast(f32),
                                        ALU.subtract).then_inc(s_hlo, 1)

            def thresholds(m):
                dve.wait_ge(s_sum, m + 1)
                nc.vector.tensor_reduce(w_sum[:, m:m + 1], bank[SUM_BANK][:, 0:NCH], AX.X,
                                        ALU.add).then_inc(s_wsum, 1)
                dve.wait_ge(s_wsum, m + 1)
                ps = w_sum[:, m:m + 1]
                if m == DOWN:
                    nc.vector.tensor_scalar(thr[:, m, 1:2], ps, -0.5 / COUNT, -0.5 * EPS, ALU.mult, ALU.add)
                nc.vector.tensor_scalar(thr[:, m, 0:1], ps, 0.5 / COUNT, 0.5 * EPS, ALU.mult,
                                        ALU.add).then_inc(s_thr, 1)
                dve.wait_ge(s_thr, m + 1)

            def scale_of(m):
                k = 1.0 if m == DOWN else 2.0
                nc.vector.tensor_scalar(scale[:, m:m + 1], w_sum[:, m:m + 1], k / COUNT, k * EPS, ALU.mult,
                                        ALU.add).then_inc(s_scale, 1)

            def negative_down(c):
                nc.vector.tensor_scalar(neg[:, c], chunk(w_sb[DOWN], c), thr[:, DOWN, 1:2], None,
                                        ALU.is_lt).then_inc(s_neg, 1)

            def ternary(m, c):
                if m == DOWN:
                    dve.wait_ge(s_neg, c + 1)
                    nc.vector.scalar_tensor_tensor(
                        out=chunk(tern[m], c), in0=chunk(w_sb[m], c), scalar=thr[:, m, 0:1], in1=neg[:, c],
                        op0=ALU.is_gt, op1=ALU.subtract).then_inc(s_tern, 1)
                else:
                    dve.wait_ge(s_abs, NCH * m + c + 1)
                    dve.wait_ge(s_sgn, NCH * m + c + 1)
                    nc.vector.scalar_tensor_tensor(
                        out=chunk(tern[m], c), in0=chunk(w_abs[m], c), scalar=thr[:, m, 0:1],
                        in1=chunk(w_sgn[m], c), op0=ALU.is_gt, op1=ALU.mult).then_inc(s_tern, 1)

            def query_embedding():
                dve.wait_ge(s_q, 1)
                for d in range(DT):
                    last = nc.vector.tensor_scalar(q_emb[:, d], bank[Q_BANK][:, NB * d:NB * (d + 1)],
                                                   b3_sb[:, d:d + 1], 0.0, ALU.add, ALU.max)
                last.then_inc(s_qemb, 1)
                dve.wait_ge(s_qemb, 1)

            def finish(hf):
                for n, (b, d, q0, q1) in enumerate(pieces[hf]):
                    if n == len(pieces[hf]) - 1:
                        dve.wait_ge(s_down, ET * (hf + 1))
                    else:
                        dve.wait_ge(s_y, (len(pieces[0]) - 1) * hf + n + 1)
                    nc.vector.scalar_tensor_tensor(
                        out=y_sb[:, q0:q1, d],
                        in0=bank[b][:, 0:QT * (q1 - q0)].rearrange("p (q t) -> p q t", t=QT),
                        scalar=scale[:, DOWN:DOWN + 1], in1=x_sb[:, q0:q1, d],
                        op0=ALU.mult, op1=ALU.add).then_inc(s_fin, 1)

            def hidden_low(i):
                dve.wait_ge(s_hihi, i + 1)
                nc.vector.tensor_tensor(hid_lo[:, i % RING], hid[:, i], hid_hi[:, i % RING].bitcast(f32),
                                        ALU.subtract).then_inc(s_hilo, 1)

            def hidden(i):
                dve.wait_ge(s_gate, i + 1)
                dve.wait_ge(s_silu, i + 1)
                nc.vector.scalar_tensor_tensor(
                    out=hid[:, i], in0=psum[:, i % WB], scalar=scale[:, GATE:GATE + 1], in1=hid[:, i],
                    op0=ALU.mult, op1=ALU.mult).then_inc(s_hid, 1)

            x_quarter(0)
            x_quarter(1)
            dve.wait_ge(s_w[UP][NCH - 1], 16)
            nc.vector.tensor_reduce(abs_sum[:, UP, NCH - 1:NCH], chunk(w_sb[UP], NCH - 1), AX.XYZ, ALU.add,
                                    apply_absolute_value=True).then_inc(s_abs_last, 1)
            thresholds(UP)
            split_h(0)
            ternary(UP, 0)
            scale_of(UP)
            split_h(1)
            ternary(UP, 1)
            x_quarter(2)
            ternary(UP, 2)
            x_quarter(3)
            ternary(UP, 3)
            split_h(2)
            thresholds(GATE)
            ternary(GATE, 0)
            scale_of(GATE)
            split_h(3)
            for c in range(1, NCH):
                ternary(GATE, c)
            thresholds(DOWN)
            negative_down(0)
            scale_of(DOWN)
            for c in range(NCH):
                if c + 1 < NCH:
                    negative_down(c + 1)
                ternary(DOWN, c)
            hidden(0)
            with dve.Fori(1, ET + LAG) as i:
                hidden(i)
                hidden_low(i - 1)
            finish(0)
            with dve.Fori(ET + LAG, STEPS) as i:
                hidden(i)
                hidden_low(i - 1)
            hidden_low(STEPS - 1)
            finish(1)

        @block.tensor
        def _(pe):
            def sum_matrix(m):
                if m == UP:
                    pe.wait_ge(s_abs, NCH - 1)
                    pe.wait_ge(s_abs_last, 1)
                else:
                    pe.wait_ge(s_abs, NCH * (m + 1))
                    pe.wait_ge(s_wsum, m)
                nc.tensor.matmul(bank[SUM_BANK][:, 0:NCH], ones[:], abs_sum[:, m], start=True,
                                 stop=True).then_inc(s_sum, 1)

            def w2_quarter(q):
                pe.wait_ge(s_xc, q + 1)
                for d in range(DT):
                    if q == 3 and d == 1:
                        pe.wait_ge(s_h, DT * 2 + 1)
                    for k in range(DT):
                        last = nc.tensor.matmul(bank[w2_bank[q][d]][:, 0:QT], w2_sb[:, k, P * d:P * (d + 1)],
                                                xc[:, q, k], start=(k == 0), stop=(k == DT - 1))
                        if q == 1 and d == 0 and k == 0:
                            sum_matrix(UP)
                    last.then_inc(s_hp, 1)

            def h_tile(m, i, out, qs):
                n = 0
                for k in range(DT):
                    for part in (h_hi, h_lo):
                        last = nc.tensor.matmul(out, tern[m][:, i % ET, k], part[:, k, qs],
                                                start=(n == 0), stop=(n == 2 * DT - 1))
                        n += 1
                return last

            def up(i):
                if i == ET:
                    pe.wait_ge(s_hlo, NQ)
                if i < ET and i % CT == 0:
                    pe.wait_ge(s_tern, i // CT + 1)
                if i >= WB:
                    pe.wait_ge(s_silu, i - WB + 1)
                h_tile(UP, i, bank[i % WB][:, :], HALVES[i // ET]).then_inc(s_up, 1)

            def gate(i):
                if i < ET and i % CT == 0:
                    pe.wait_ge(s_tern, NCH + i // CT + 1)
                if i < WB:
                    pe.wait_ge(s_silu, STEPS - WB + i + 1)
                else:
                    pe.wait_ge(s_hid, i - WB + 1)
                h_tile(GATE, i, bank[i % WB][:, :], HALVES[i // ET]).then_inc(s_gate, 1)

            def down(i, n):
                hf, e = divmod(i, ET)
                b, d, q0, q1 = pieces[hf][n]
                if n == 0:
                    pe.wait_ge(s_hilo, i + 1)
                    if hf == 0 and e % CT == 0:
                        pe.wait_ge(s_tern, 2 * NCH + e // CT + 1)
                before = [p[0] for p in pieces[0]]
                if hf == 1 and e == 0 and b in before:
                    pe.wait_ge(s_fin, before.index(b) + 1)
                ts = slice(QT * (q0 % 2), QT * (q0 % 2 + q1 - q0))
                for k, part in enumerate((hid_hi, hid_lo)):
                    last = nc.tensor.matmul(bank[b][:, 0:QT * (q1 - q0)], tern[DOWN][:, e, d],
                                            part[:, i % RING, ts], start=(e == 0 and k == 0),
                                            stop=(e == ET - 1 and k == 1))
                if n == len(pieces[hf]) - 1:
                    last.then_inc(s_down, 1)
                elif e == ET - 1:
                    last.then_inc(s_y, 1)

            def warm_up():
                nc.tensor.matmul(bank[WARM_BANK][:, :], warm[:, 0:P], warm[:, :], start=True, stop=True)

            pe.wait_ge(s_const, 1)
            for _ in range(6):
                warm_up()
            pe.wait_ge(s_small, 16)
            for d in range(DT):
                last = nc.tensor.matmul(bank[Q_BANK][:, NB * d:NB * (d + 1)], w3_sb[:, P * d:P * (d + 1)],
                                        cond_sb, start=True, stop=True)
            last.then_inc(s_q, 1)
            for _ in range(4):
                warm_up()
            pe.wait_ge(s_w2, 16)
            w2_quarter(0)
            w2_quarter(1)
            for _ in range(2):
                warm_up()
            for q in range(2):
                pe.wait_ge(s_hlo, q + 1)
                pe.wait_ge(s_tern, 1)
                for i in range(2):
                    last = h_tile(UP, i, bank[i % WB][:, QT * q:QT * (q + 1)], q)
                    if q:
                        last.then_inc(s_up, 1)
            up(2)
            up(3)
            w2_quarter(2)
            up(4)
            sum_matrix(GATE)
            w2_quarter(3)
            up(5)
            up(6)
            up(7)
            for i in range(8, STEPS):
                up(i)
                if i == 9:
                    sum_matrix(DOWN)
            for i in range(STEPS):
                gate(i)
                if i == ET + LAG + 1:
                    down(ET, 2)
                if i >= LAG:
                    for n in range(len(pieces[(i - LAG) // ET])):
                        if (i - LAG, n) != (ET, 2):
                            down(i - LAG, n)
            for i in range(STEPS - LAG, STEPS - 1):
                down(i, 0)
                down(i, 1)
            down(STEPS - LAG, 2)
            down(STEPS - 1, 0)
            down(STEPS - 1, 1)
            for i in range(STEPS - LAG + 1, STEPS):
                down(i, 2)


def kernel(x, cond_1024, L0_cond_W3, L0_cond_b3, L0_cond_W2, L0_cond_b2, L0_ffn_W_up, L0_ffn_W_gate, L0_ffn_W_down):
    import numpy as np
    import concourse.bacc as bacc
    from concourse import mybir
    from concourse.bass_utils import run_bass_kernel_spmd

    P, NQ, DT = 128, 4, 2
    B, N, D = x.shape
    E = L0_ffn_W_up.shape[0]
    QT = B * N // NQ
    ET = E // P

    def lay(a):
        return np.ascontiguousarray(a)

    arrays = {
        "x_t": lay(np.asarray(x).reshape(NQ, QT, DT, P).transpose(3, 0, 2, 1)),
        "small": lay(np.concatenate([np.asarray(L0_cond_W3), np.asarray(cond_1024).T,
                                     np.asarray(L0_cond_b3).reshape(DT, P).T,
                                     np.asarray(L0_cond_b2).reshape(DT, P).T], axis=1)),
        "w2": lay(np.asarray(L0_cond_W2).reshape(DT, P, D).transpose(1, 0, 2)),
        "w_up": lay(np.asarray(L0_ffn_W_up).reshape(ET, P, DT, P).transpose(3, 0, 2, 1)),
        "w_gate": lay(np.asarray(L0_ffn_W_gate).reshape(ET, P, DT, P).transpose(3, 0, 2, 1)),
        "w_down": lay(np.asarray(L0_ffn_W_down).reshape(DT, P, ET, P).transpose(3, 2, 0, 1)),
    }
    nc = bacc.Bacc("TRN2", target_bir_lowering=False, num_devices=1)
    args = [nc.dram_tensor(name, a.shape, mybir.dt.from_np(a.dtype), kind="ExternalInput").ap()
            for name, a in arrays.items()]
    y = nc.dram_tensor("y_t", (P, NQ, DT, QT), mybir.dt.float32, kind="ExternalOutput").ap()
    adaln_ffn_kernel(nc, *args, y)
    got = run_bass_kernel_spmd(nc, [arrays], core_ids=[0]).results[0]["y_t"]
    return lay(got.transpose(1, 3, 2, 0)).reshape(B, N, D)
```
